# Optimizing a Trainium2 kernel written in Bass

```python
import numpy as np
import jax
import jax.numpy as jnp

def _softmax(x, axis=-1):
    return jax.nn.softmax(x, axis=axis)

def _gelu(x):
    return jax.nn.gelu(x, approximate=True)

def _silu(x):
    return jax.nn.silu(x)

def _sigmoid(x):
    return jax.nn.sigmoid(x)

def _layernorm(x, axis=-1, eps=1e-05):
    m = jnp.mean(x, axis=axis, keepdims=True)
    v = jnp.var(x, axis=axis, keepdims=True)
    return (x - m) / jnp.sqrt(v + eps)

def _scatter_add(tgt, idx, src, axis=0):
    return tgt.at[idx].add(src)

def _segment_sum(src, seg, n):
    return jax.ops.segment_sum(src, seg, n)
kernel_name = 'mk_adaln_d1_jaxref_r8_68093b'

def setup_inputs(seed: int=0):
    np.random.seed(seed)
    _w = jnp.asarray

    def _L0_attn_setup():
        import jax, jax.numpy as jnp
        import numpy as np
        B, S, D_IN, D_OUT = (4, 256, 128, 128)
        key = jax.random.key(seed)
        ks = jax.random.split(key, 7)
        scale = 1.0 / np.sqrt(D_IN)
        x = jax.random.normal(ks[0], (B, S, D_IN), dtype=jnp.float32)
        Wq = jax.random.uniform(ks[1], (D_IN, D_OUT), jnp.float32, -scale, scale)
        bq = jax.random.uniform(ks[2], (D_OUT,), jnp.float32, -scale, scale)
        Wk = jax.random.uniform(ks[3], (D_IN, D_OUT), jnp.float32, -scale, scale)
        bk = jax.random.uniform(ks[4], (D_OUT,), jnp.float32, -scale, scale)
        Wv = jax.random.uniform(ks[5], (D_IN, D_OUT), jnp.float32, -scale, scale)
        bv = jax.random.uniform(ks[6], (D_OUT,), jnp.float32, -scale, scale)
        return {'x': x, 'Wq': Wq, 'bq': bq, 'Wk': Wk, 'bk': bk, 'Wv': Wv, 'bv': bv}
    _L0_attn_in = _L0_attn_setup()

    def _L0_ffn_setup():
        import jax, jax.numpy as jnp
        import numpy as np
        DIM = 128
        DEPTH = 6
        HEADS = 16
        DIM_HEAD = 64
        WINDOW = 32
        INNER = HEADS * DIM_HEAD
        DIM_INNER = int(DIM * 4 * 2 / 3)
        QK_SCALE = 8.0

        def shift_tokens(t):
            a, s = jnp.split(t, 2, -1)
            s = jnp.pad(s, ((0, 0), (1, 0), (0, 0)))[:, :-1]
            return jnp.concatenate([a, s], -1)

        def l2norm(t):
            return t / jnp.maximum(jnp.linalg.norm(t, axis=-1, keepdims=True), 1e-12)

        def rotate_half(x):
            x1, x2 = jnp.split(x, 2, -1)
            return jnp.concatenate([-x2, x1], -1)

        def rotary_tables(n):
            half = jnp.arange(0, DIM_HEAD, 2, dtype=jnp.float32)
            inv_freq = 1.0 / 10000.0 ** (half / DIM_HEAD)
            t = jnp.arange(n, dtype=jnp.float32)
            freqs = t[:, None] * inv_freq[None, :]
            freqs = jnp.concatenate([freqs, freqs], -1)
            base_scale = (half + 0.4 * DIM_HEAD) / (1.4 * DIM_HEAD)
            power = (t - n // 2) / (WINDOW // 2)
            scale = base_scale[None, :] ** power[:, None]
            scale = jnp.concatenate([scale, scale], -1)
            return (freqs, scale)

        def local_attention(q, k, v):
            b, h, n, d = q.shape
            w = WINDOW
            nw = n // w
            bq = q.reshape(b, h, nw, w, d)
            bk = k.reshape(b, h, nw, w, d)
            bv = v.reshape(b, h, nw, w, d)

            def look(t):
                p = jnp.pad(t, ((0, 0), (0, 0), (1, 0), (0, 0), (0, 0)))
                return jnp.concatenate([p[:, :, :nw], p[:, :, 1:]], axis=3)
            bk2, bv2 = (look(bk), look(bv))
            seq = jnp.arange(n).reshape(nw, w)
            seq_p = jnp.pad(seq, ((1, 0), (0, 0)), constant_values=-1)
            jt = jnp.concatenate([seq_p[:nw], seq_p[1:]], axis=1)
            it = seq[:, :, None]
            jb = jt[:, None, :]
            mask = (it < jb) | (it > jb + w) | (jb == -1)
            sim = jnp.einsum('bhwie,bhwje->bhwij', bq, bk2) * QK_SCALE
            sim = jnp.where(mask, -jnp.finfo(sim.dtype).max, sim)
            attn = jax.nn.softmax(sim, -1)
            out = jnp.einsum('bhwij,bhwje->bhwie', attn, bv2)
            return out.reshape(b, h, n, d)

        def attn_layer(x, Wqkv, qs, ksc, Wo):
            b, n, _ = x.shape
            qkv = x @ Wqkv
            q, k, v = jnp.split(qkv, 3, -1)
            sh = lambda t: t.reshape(b, n, HEADS, DIM_HEAD).transpose(0, 2, 1, 3)
            q, k, v = (sh(q), sh(k), sh(v))
            q = l2norm(q) * qs
            k = l2norm(k) * ksc
            freqs, scale = rotary_tables(n)
            cos, sin = (jnp.cos(freqs), jnp.sin(freqs))
            q = q * cos * scale + rotate_half(q) * sin * scale
            inv = 1.0 / scale
            k = k * cos * inv + rotate_half(k) * sin * inv
            out = local_attention(q, k, v)
            out = out.transpose(0, 2, 1, 3).reshape(b, n, INNER)
            return out @ Wo

        def ffn_layer(x, g, bln, W1, b1, W2, b2):
            mu = x.mean(-1, keepdims=True)
            var = ((x - mu) ** 2).mean(-1, keepdims=True)
            xn = (x - mu) / jnp.sqrt(var + 1e-05) * g + bln
            hg = xn @ W1 + b1
            a, gate = jnp.split(hg, 2, -1)
            return a * jax.nn.gelu(gate, approximate=False) @ W2 + b2
        key = jax.random.key(seed)
        ks = jax.random.split(key, 8)
        B, N = (2, 256)
        init = lambda k, shape: jax.random.normal(k, shape, jnp.float32) * 0.02
        return {'x': jax.random.normal(ks[0], (B, N, DIM), jnp.float32), 'Wqkv': init(ks[1], (DEPTH, DIM, 3 * INNER)), 'q_scale': jnp.ones((DEPTH, DIM_HEAD), jnp.float32), 'k_scale': jnp.ones((DEPTH, DIM_HEAD), jnp.float32), 'Wo': init(ks[2], (DEPTH, INNER, DIM)), 'ln_g': jnp.ones((DEPTH, DIM), jnp.float32), 'ln_b': jnp.zeros((DEPTH, DIM), jnp.float32), 'W1': init(ks[3], (DEPTH, DIM, 2 * DIM_INNER)), 'b1': jnp.zeros((DEPTH, 2 * DIM_INNER), jnp.float32), 'W2': init(ks[4], (DEPTH, DIM_INNER, DIM)), 'b2': jnp.zeros((DEPTH, DIM), jnp.float32)}
    _L0_ffn_in = _L0_ffn_setup()
    _L0_c = _w((lambda *s: np.random.randn(*s).astype(np.float32) * 0.05)(4, 128))
    _L0_wmod = _w((lambda *s: np.random.randn(*s).astype(np.float32) * 0.05)(128, 6 * 128) * 128 ** (-0.5))
    _d = {'L0_attn_x': _L0_attn_in['x'], 'L0_attn_Wq': _L0_attn_in['Wq'], 'L0_attn_bq': _L0_attn_in['bq'], 'L0_attn_Wk': _L0_attn_in['Wk'], 'L0_attn_bk': _L0_attn_in['bk'], 'L0_attn_Wv': _L0_attn_in['Wv'], 'L0_attn_bv': _L0_attn_in['bv'], 'L0_ffn_Wqkv': _L0_ffn_in['Wqkv'], 'L0_ffn_q_scale': _L0_ffn_in['q_scale'], 'L0_ffn_k_scale': _L0_ffn_in['k_scale'], 'L0_ffn_Wo': _L0_ffn_in['Wo'], 'L0_ffn_ln_g': _L0_ffn_in['ln_g'], 'L0_ffn_ln_b': _L0_ffn_in['ln_b'], 'L0_ffn_W1': _L0_ffn_in['W1'], 'L0_ffn_b1': _L0_ffn_in['b1'], 'L0_ffn_W2': _L0_ffn_in['W2'], 'L0_ffn_b2': _L0_ffn_in['b2'], 'L0_c': _L0_c, 'L0_wmod': _L0_wmod}
    _x0 = _d['L0_attn_x']
    _d['L0_attn_x'] = jax.random.normal(jax.random.fold_in(jax.random.key(seed), 1), (4, 1024, 128), dtype=_x0.dtype)
    del _x0
    return _d

def reference(L0_attn_x, L0_attn_Wq, L0_attn_bq, L0_attn_Wk, L0_attn_bk, L0_attn_Wv, L0_attn_bv, L0_ffn_Wqkv, L0_ffn_q_scale, L0_ffn_k_scale, L0_ffn_Wo, L0_ffn_ln_g, L0_ffn_ln_b, L0_ffn_W1, L0_ffn_b1, L0_ffn_W2, L0_ffn_b2, L0_c, L0_wmod):

    def _L0_attn_ref(x, Wq, bq, Wk, bk, Wv, bv):
        import jax, jax.numpy as jnp
        import numpy as np
        B, S, D_IN, D_OUT = (4, 256, 128, 128)
        q = jnp.einsum('bsd,df->bsf', x, Wq) + bq
        k = jnp.einsum('bsd,df->bsf', x, Wk) + bk
        v = jnp.einsum('bsd,df->bsf', x, Wv) + bv
        inv_sqrt_d = 1.0 / jnp.sqrt(jnp.asarray(q.shape[-1], q.dtype))
        scores = jnp.einsum('bqf,bkf->bqk', q, k) * inv_sqrt_d
        attn = jax.nn.softmax(scores, axis=-1)
        return jnp.einsum('bqk,bkf->bqf', attn, v)

    def _L0_ffn_ref(x, Wqkv, q_scale, k_scale, Wo, ln_g, ln_b, W1, b1, W2, b2):
        import jax, jax.numpy as jnp
        import numpy as np
        DIM = 128
        DEPTH = 6
        HEADS = 16
        DIM_HEAD = 64
        WINDOW = 32
        INNER = HEADS * DIM_HEAD
        DIM_INNER = int(DIM * 4 * 2 / 3)
        QK_SCALE = 8.0

        def shift_tokens(t):
            a, s = jnp.split(t, 2, -1)
            s = jnp.pad(s, ((0, 0), (1, 0), (0, 0)))[:, :-1]
            return jnp.concatenate([a, s], -1)

        def l2norm(t):
            return t / jnp.maximum(jnp.linalg.norm(t, axis=-1, keepdims=True), 1e-12)

        def rotate_half(x):
            x1, x2 = jnp.split(x, 2, -1)
            return jnp.concatenate([-x2, x1], -1)

        def rotary_tables(n):
            half = jnp.arange(0, DIM_HEAD, 2, dtype=jnp.float32)
            inv_freq = 1.0 / 10000.0 ** (half / DIM_HEAD)
            t = jnp.arange(n, dtype=jnp.float32)
            freqs = t[:, None] * inv_freq[None, :]
            freqs = jnp.concatenate([freqs, freqs], -1)
            base_scale = (half + 0.4 * DIM_HEAD) / (1.4 * DIM_HEAD)
            power = (t - n // 2) / (WINDOW // 2)
            scale = base_scale[None, :] ** power[:, None]
            scale = jnp.concatenate([scale, scale], -1)
            return (freqs, scale)

        def local_attention(q, k, v):
            b, h, n, d = q.shape
            w = WINDOW
            nw = n // w
            bq = q.reshape(b, h, nw, w, d)
            bk = k.reshape(b, h, nw, w, d)
            bv = v.reshape(b, h, nw, w, d)

            def look(t):
                p = jnp.pad(t, ((0, 0), (0, 0), (1, 0), (0, 0), (0, 0)))
                return jnp.concatenate([p[:, :, :nw], p[:, :, 1:]], axis=3)
            bk2, bv2 = (look(bk), look(bv))
            seq = jnp.arange(n).reshape(nw, w)
            seq_p = jnp.pad(seq, ((1, 0), (0, 0)), constant_values=-1)
            jt = jnp.concatenate([seq_p[:nw], seq_p[1:]], axis=1)
            it = seq[:, :, None]
            jb = jt[:, None, :]
            mask = (it < jb) | (it > jb + w) | (jb == -1)
            sim = jnp.einsum('bhwie,bhwje->bhwij', bq, bk2) * QK_SCALE
            sim = jnp.where(mask, -jnp.finfo(sim.dtype).max, sim)
            attn = jax.nn.softmax(sim, -1)
            out = jnp.einsum('bhwij,bhwje->bhwie', attn, bv2)
            return out.reshape(b, h, n, d)

        def attn_layer(x, Wqkv, qs, ksc, Wo):
            b, n, _ = x.shape
            qkv = x @ Wqkv
            q, k, v = jnp.split(qkv, 3, -1)
            sh = lambda t: t.reshape(b, n, HEADS, DIM_HEAD).transpose(0, 2, 1, 3)
            q, k, v = (sh(q), sh(k), sh(v))
            q = l2norm(q) * qs
            k = l2norm(k) * ksc
            freqs, scale = rotary_tables(n)
            cos, sin = (jnp.cos(freqs), jnp.sin(freqs))
            q = q * cos * scale + rotate_half(q) * sin * scale
            inv = 1.0 / scale
            k = k * cos * inv + rotate_half(k) * sin * inv
            out = local_attention(q, k, v)
            out = out.transpose(0, 2, 1, 3).reshape(b, n, INNER)
            return out @ Wo

        def ffn_layer(x, g, bln, W1, b1, W2, b2):
            mu = x.mean(-1, keepdims=True)
            var = ((x - mu) ** 2).mean(-1, keepdims=True)
            xn = (x - mu) / jnp.sqrt(var + 1e-05) * g + bln
            hg = xn @ W1 + b1
            a, gate = jnp.split(hg, 2, -1)
            return a * jax.nn.gelu(gate, approximate=False) @ W2 + b2
        for i in range(DEPTH):
            x = attn_layer(shift_tokens(x), Wqkv[i], q_scale[i], k_scale[i], Wo[i]) + x
            x = ffn_layer(shift_tokens(x), ln_g[i], ln_b[i], W1[i], b1[i], W2[i], b2[i]) + x
        return x
    x = L0_attn_x
    mod = (_silu(L0_c) @ L0_wmod).reshape(L0_c.shape[0], 6, 1, -1)
    sa, ca, ga, sb, cb, gb = (mod[:, 0], mod[:, 1], mod[:, 2], mod[:, 3], mod[:, 4], mod[:, 5])
    ga = (2 * (ga >= 0) - 1) * jnp.maximum(jnp.abs(ga), 0.25)
    gb = (2 * (gb >= 0) - 1) * jnp.maximum(jnp.abs(gb), 0.25)
    h = _layernorm(x, axis=-1) * (1 + ca) + sa
    x = x + ga * _L0_attn_ref(h, L0_attn_Wq, L0_attn_bq, L0_attn_Wk, L0_attn_bk, L0_attn_Wv, L0_attn_bv)
    h = _layernorm(x, axis=-1) * (1 + cb) + sb
    x = x + gb * _L0_ffn_ref(h, L0_ffn_Wqkv, L0_ffn_q_scale, L0_ffn_k_scale, L0_ffn_Wo, L0_ffn_ln_g, L0_ffn_ln_b, L0_ffn_W1, L0_ffn_b1, L0_ffn_W2, L0_ffn_b2)
    return x

_drawn_inputs = setup_inputs


def setup_inputs(seed=0):
    import zlib

    import numpy as np

    out = dict(_drawn_inputs(seed))
    spreads = {'L0_ffn_q_scale': (1.0, 0.6),
     'L0_ffn_k_scale': (1.0, 0.6),
     'L0_ffn_ln_g': (1.0, 0.6),
     'L0_ffn_ln_b': (0.0, 0.8),
     'L0_ffn_b1': (0.0, 0.8),
     'L0_ffn_b2': (0.0, 0.649)}
    factors = {'L0_attn_Wq': 8.0,
     'L0_attn_bq': 8.0,
     'L0_attn_Wk': 8.0,
     'L0_attn_bk': 64.0,
     'L0_attn_Wv': 8.0,
     'L0_attn_bv': 4.291,
     'L0_ffn_W1': 7.38,
     'L0_ffn_W2': 7.248}
    for name, (base, spread) in spreads.items():
        noise = np.random.default_rng([zlib.crc32(name.encode()), seed]).standard_normal(out[name].shape)
        drawn = base * np.exp(spread * noise) if base else spread * noise
        out[name] = jnp.asarray(drawn.astype(out[name].dtype))
    for name, factor in factors.items():
        out[name] = (out[name] * factor).astype(out[name].dtype)
    return out
```

```python
from contextlib import ExitStack

import concourse.bass as bass
from concourse import mybir

F32 = mybir.dt.float32
BF16 = mybir.dt.bfloat16
F32R = mybir.dt.float32r
ALU = mybir.AluOpType
ACT = mybir.ActivationFunctionType
AX = mybir.AxisListType

P = 128
B, S, D = 4, 1024, 128
DEPTH, HEADS, DH, WIN = 6, 16, 64, 32
INNER = HEADS * DH
DFF = int(D * 4 * 2 / 3)
QK_SCALE = 8.0
TOK = B * S
TILES = TOK // P
TPB = S // P
GPT = HEADS // 4
GROUPS = TILES * GPT
UNROLL = 2 * GPT
ITERS = GROUPS // UNROLL
KEYS = 3 * WIN
PITCH = S + 1
HIST = WIN + 1
CH = 3
CW = [P, P, DFF - 2 * P]
BLK = 512
BLOCKS = TOK // BLK
NEG = -1.0e30
LNEPS = 1e-5
PARTS = ((0, 0), (0, 1), (1, 0))
RN_SCALE = 256.0


def build(nc, x, w_attn, b_qk, b_v, Wqkv, Wo, W1, W2, cols, b1_cols, gains, c_t, wmod, rot_tab, out):
    ctx = ExitStack()
    with ctx:
        def sb(name, shape, dt=F32):
            return ctx.enter_context(nc.sbuf_tensor(name, shape, dt))

        def sem(name):
            return ctx.enter_context(nc.semaphore(name))

        psum = ctx.enter_context(nc.psum_tensor("psum", [P, 8, 512], F32))
        bank = [psum[:, i, :] for i in range(8)]

        ident = sb("ident", [P, P])
        ident_bf = sb("ident_bf", [P, P], BF16)
        mask = sb("mask", [P, 4, 2, KEYS], BF16)
        minus_half = sb("minus_half", [P, TPB])
        keep = sb("keep", [P, 4, 2, WIN])
        eps_row = sb("eps_row", [P, TPB])
        wa = sb("wa", [P, 3, D])
        wmod_sb = sb("wmod_sb", [P, 6 * D])
        bqk_col = sb("bqk_col", [P, 2])
        bv_row = sb("bv_row", [P, D])
        c_col = sb("c_col", [P, B])
        silu_t = sb("silu_t", [P, 3, B])
        silu_wide = sb("silu_wide", [P, B, P])
        mod_col = sb("mod_col", [P, 6, B])
        ga_row = sb("ga_row", [P, B, D])
        yT = sb("yT", [P, 2, BLK])
        clamp_t = yT
        clamp_c = sb("clamp_c", [P, 2, B])
        rot_raw = sb("rot_raw", [P, TPB, 2, 2, DH])
        rot = sb("rot", [P, 2, TPB, 2, DH])
        qk_gain = sb("qk_gain", [P, DEPTH, 2, 2, DH])
        wqkv = sb("wqkv", [P, 3, INNER])
        whi = sb("whi", [P, 3, INNER], F32R)
        wlo = sb("wlo", [P, 3, INNER], F32R)
        wparts = (whi, wlo)
        wo = sb("wo", [P, INNER // P, D])
        w1 = sb("w1", [P, 2 * DFF])
        w2 = sb("w2", [P, CH, D])
        b1_col = sb("b1_col", [P, DEPTH, 2, CH])
        vec_cols = sb("vec_cols", [P, 3, DEPTH])
        lng_col, lnb_col, b2_col = (vec_cols[:, i, :] for i in range(3))

        xtok = sb("xtok", [P, TILES, D])
        xs_in = sb("xs_in", [P, HIST - 1 + B * PITCH])
        x_mid = sb("x_mid", [P, B * PITCH])

        xsh = sb("xsh", [P, 2, WIN + P])
        work = sb("work", [P, 4, 8, DH])
        sq, qkn, rcos, rsin = (work[:, i, :, :] for i in range(4))
        ssq = sb("ssq", [P, 8])
        ssg = sb("ssg", [P, 8])
        lnss = sb("lnss", [P, 8])
        rnorm = sb("rnorm", [P, 8])
        qkr = sb("qkr", [P, 512])
        qbd = sb("qbd", [P, 2, 2, 2, DH])
        kT = sb("kT", [P, HEADS // 2, WIN + P])
        nmax = sb("nmax", [P, 4])
        prob = sb("prob", [P, 2, 4, KEYS])
        probT = sb("probT", [KEYS, 4, P])
        vs = sb("vs", [KEYS, 2, 2, 4, DH])
        psumr = sb("psumr", [P, 2, 2, 4])
        probn = sb("probn", [P, 4, KEYS])
        aoT = sb("aoT", [P, 2, INNER // P, P])

        xhi = sb("xhi", [P, 2, WIN + P], F32R)
        xlo = sb("xlo", [P, 2, WIN + P], F32R)
        xparts = (xhi, xlo)

        xf = sb("xf", [P, BLK])
        st6 = sb("st6", [P, TPB, 6])
        mv = sb("mv", [P, TPB, 2])
        vare = sb("vare", [P, TPB])
        rstd = sb("rstd", [P, TPB])
        xn = sb("xn", [P, TPB, D])
        xnT = sb("xnT", [P, BLK])
        gel = sb("gel", [P, 2, BLK])
        uT = sb("uT", [P, CH, BLK])

        yout = sb("yout", [P, 2, 4, D])
        hT, qT, kgT = (wqkv[:, i, :] for i in range(3))
        vg = sb("vg", [P, TPB, D])
        pg = work[:, :, :, :].rearrange("p (h a) b d -> p h (a b d)", h=2)
        pgT = yout[:, :, :, :].rearrange("p h a d -> p (h a) d")
        gmax = sb("gmax", [P, 2, 2])
        gsum = sb("gsum", [P, 2, 2])

        names = """x_in small_in const_in gain_in ones_ready id_zero id_ready mask_ready pad_ready
            silu_step silu_ready wide_ready modp_ready mod_ready gap_ready clamp_step
            gst_step gmv_ready gve_step grstd_ready gxn_ready gtr_ready gh_ready gq_ready gqk_ready gv_ready gvt_step gvs_ready
            gs_ready gm_step gm_ready ge_ready gt_ready gte_a gte_d go_ready gri_step gx_ready
            wqkv_in wo_in w1_in w2_in
            proj_ready sq_ready ss_ready sg_ready ln_ready rn_ready qkn_ready rot_ready qkr_ready tr_ready
            qk_ready sim_ready max_ready p_ready pt_ready pts_ready vp_ready vs_ready pv_ready
            ri_ready aot_ready wo_ready x_mid_ready tail_ready gain_ready pn_ready xs_ready xh_step w_split sum_ready
            f_x f_tr f_mvs f_mv f_ve f_rstd f_xn f_trn f_xnT f_gate f_a f_gel f_u f_y f_out
            y_ready y_tr yo_ready y_sent""".split()
        s = {n: sem(n) for n in names}

        xsh_in = [sem(f"xsh_in{tp}") for tp in range(2)]
        counts_of = {}
        block = ctx.enter_context(nc.Block())

        def need(eng, what, base, off, first=False):
            if first and off <= 0:
                return
            eng.wait_ge(s[what], base + off)

        def need_tiles(eng, what, layer, it, tile_off, first, last):
            if first and tile_off < 0:
                return
            tiles = layer * TILES + (TILES if last else it * 2)
            eng.wait_ge(s[what], tiles + tile_off + 1)

        def prep_main(eng, prep, main, kb, odd):
            main(kb, odd)
            prep(kb + 1)

        def wait_apart(eng, *waits):
            for k, (what, value) in enumerate(waits):
                eng.reg_mov(counts_of[eng.engine][k], value)
            eng.wait_ge(s["id_ready"], 1)
            for k, (what, value) in enumerate(waits):
                eng.wait_ge(s[what], counts_of[eng.engine][k])

        def attention_bodies(eng, layer, body):
            body(eng.snap(layer * GROUPS), 0, True, False)
            with eng.Fori(1, ITERS) as it:
                body(eng.snap(layer * GROUPS + it * UNROLL), it, False, False)
            body(eng.snap(layer * GROUPS + GROUPS), 0, False, True)

        def group_of(u, lag, first, last):
            j = u - lag
            if (first and j < 0) or (last and j >= 0):
                return None
            return j

        @block.sync
        def _(sp):
            for b in range(B):
                sp.dma_start(xtok[:, b * TPB:(b + 1) * TPB, :],
                             x[b].rearrange("(t p) d -> p t d", p=P)).then_inc(s["x_in"], 16)

            def load_attention(layer):
                sp.dma_start(wqkv[:, :, :].rearrange("p k n -> p (k n)"), Wqkv[layer]).then_inc(s["wqkv_in"], 16)
                sp.dma_start(wo[:, :, :].rearrange("p k n -> p (k n)"), Wo[layer]).then_inc(s["wo_in"], 16)

            def load_ffn(layer):
                sp.dma_start(w1[:, :], W1[layer]).then_inc(s["w1_in"], 16)
                sp.dma_start(w2[:, :, :].rearrange("p k n -> p (k n)"), W2[layer]).then_inc(s["w2_in"], 16)

            counts = [sp.alloc_register(f"sp_count{k}") for k in range(3)]

            def wait_all(*waits):
                for k, (what, value) in enumerate(waits):
                    sp.reg_mov(counts[k], value)
                sp.wait_ge(s["id_ready"], 1)
                for k, (what, value) in enumerate(waits):
                    sp.wait_ge(s[what], counts[k])

            def shifted(dst, src, col, width, signal, *waits):
                wait_all(*waits)
                sp.dma_start(dst[0:64], src[0:64, bass.ds(col, width)]).then_inc(signal, 16)
                sp.dma_start(dst[64:P], src[64:P, bass.ds(col - 1, width)]).then_inc(signal, 16)

            def shift_tile(layer, it, tp, first):
                shifted(xsh[:, tp, :], xs_in, (it * 2 + tp) * P + it // (TPB // 2) + HIST - WIN, WIN + P, xsh_in[tp],
                        *([] if first else [("xs_ready", layer * TILES + it * 2 + (tp - 1))]))

            def layer_inputs(layer, last):
                wait_all(("f_out", layer * BLOCKS), ("xs_ready", layer * TILES))
                for tp in range(2):
                    shift_tile(layer, 0, tp, True)
                with sp.Fori(1, ITERS) as it:
                    for tp in range(2):
                        shift_tile(layer, it, tp, False)
                if not last:
                    wait_all(("proj_ready", layer * GROUPS + GROUPS), ("vp_ready", layer * GROUPS + GROUPS),
                             ("wo_ready", layer * TILES + TILES))
                    load_attention(layer + 1)
                with sp.Fori(0, BLOCKS) as kb:
                    shifted(xf, x_mid, kb * BLK + kb // 2 + 1, BLK, s["f_x"],
                            ("x_mid_ready", layer * TILES + kb * 4 + 4), ("f_tr", layer * BLOCKS + kb))
                if not last:
                    wait_all(("f_y", layer * BLOCKS + BLOCKS))
                    load_ffn(layer + 1)

            load_ffn(0)
            sp.wait_ge(s["gh_ready"], 4 * B)
            sp.wait_ge(s["pad_ready"], 1)
            load_attention(0)
            with sp.Fori(0, DEPTH - 1) as layer:
                layer_inputs(layer, False)
            layer_inputs(DEPTH - 1, True)

            out_v = out.rearrange("b (k t p) d -> (b k) p t d", t=4, p=P)
            with sp.Fori(0, BLOCKS // 2) as i:
                for h in range(2):
                    sp.wait_ge(s["yo_ready"], i * 2 + h + 1)
                    sp.dma_start(out_v[i * 2 + h], yout[:, h, :, :]).then_inc(s["y_sent"], 16)
            sp.wait_ge(s["y_sent"], 16 * BLOCKS)

        @block.gpsimd
        def _(pool):
            counts_of[pool.engine] = [pool.alloc_register(f"pool_count{k}") for k in range(2)]
            pool.memset(ident[:, :], 0.0).then_inc(s["id_zero"], 1)
            pool.wait_ge(s["id_zero"], 1)
            pool.affine_select(out=ident[:, :], in_=ident[:, :], compare_op=ALU.not_equal, fill=1.0, base=0,
                               pattern=[[-1, P]], channel_multiplier=1).then_inc(s["id_zero"], 1)
            pool.wait_ge(s["id_zero"], 2)
            pool.tensor_copy(ident_bf[:, :], ident[:, :]).then_inc(s["id_ready"], 1)
            pool.memset(minus_half[:, :], -0.5).then_inc(s["ones_ready"], 1)
            pool.memset(uT[:, :, :], 0.0)
            pool.memset(xs_in[:, 0:HIST], 0.0)
            pool.memset(xs_in[:, HIST + S:HIST + 3 * PITCH:PITCH], 0.0)
            pool.memset(kT[:, :, 0:WIN], 0.0)
            pool.memset(qbd[:, :, :, :, :], 0.0)
            pool.memset(keep[:, 0:3, :, :], 1.0)
            pool.memset(keep[:, 3, :, :], 0.0)
            pool.memset(eps_row[:, :], LNEPS)
            pool.memset(x_mid[:, 0:B * PITCH:PITCH], 0.0).then_inc(s["pad_ready"], 1)
            pool.memset(mask[:, :, :, :], 0.0).then_inc(s["mask_ready"], 1)
            pool.wait_ge(s["mask_ready"], 1)
            for h in range(2):
                m = mask[h * 64:h * 64 + 64, :, :, :].rearrange("p a b k -> p (a b) k")
                pool.affine_select(out=m, in_=m, compare_op=ALU.is_ge, fill=NEG, base=0,
                                   pattern=[[0, 8], [1, KEYS]], channel_multiplier=-1).then_inc(s["mask_ready"], 1)
                pool.wait_ge(s["mask_ready"], 2 + 2 * h)
                pool.affine_select(out=m, in_=m, compare_op=ALU.is_ge, fill=NEG, base=WIN,
                                   pattern=[[0, 8], [-1, KEYS]], channel_multiplier=1).then_inc(s["mask_ready"], 1)
                pool.wait_ge(s["mask_ready"], 3 + 2 * h)
            pool.memset(mask[:, 0, 0, 0:WIN], NEG).then_inc(s["mask_ready"], 1)

            pool.wait_ge(s["ones_ready"], 1)
            with pool.Fori(0, 2 * B) as n:
                pool.wait_ge(s["gmv_ready"], n + 1)
                pool.tensor_tensor(vare[:, :], mv[:, :, 1], eps_row[:, :], ALU.add).then_inc(s["gve_step"], 1)
                pool.wait_ge(s["gve_step"], n + 1)
                pool.tensor_tensor(rstd[:, :], vare[:, :], minus_half[:, :], ALU.pow).then_inc(s["grstd_ready"], 1)

            def attention(layer):
                def body(groups, it, first, last):
                    for u in range(UNROLL):
                        j = group_of(u, 4, first, last)
                        if j is not None:
                            need(pool, "ri_ready", groups, j + 1)
                            need(pool, "pt_ready", groups, j, first)
                            pool.tensor_tensor(probn[:, :, :], prob[:, j % 2, :, :], psumr[:, j % 2, 1, :].unsqueeze(2).to_broadcast([P, 4, KEYS]),
                                               ALU.mult).then_inc(s["pn_ready"], 1)
                        j = group_of(u, 1, first, last)
                        if j is not None:
                            need(pool, "rot_ready", groups, j + 1)
                            need(pool, "tr_ready", groups, j, first)
                            pool.tensor_tensor(qkr[:, :], rcos[:, :, :].rearrange("p a b -> p (a b)"),
                                               rsin[:, :, :].rearrange("p a b -> p (a b)"), ALU.add).then_inc(s["qkr_ready"], 1)
                        j = group_of(u, 3, first, last)
                        if j is not None:
                            g = j % GPT
                            if j // GPT % 2 == 0:
                                need(pool, "sim_ready", groups, j + 1)
                                kept = keep[:, 0, :, :]
                            else:
                                wait_apart(pool, ("sim_ready", groups + (j + 1)))
                                kept = keep[:, bass.ds((it + (3 if j < 0 else 0)) % 4, 1), :, :].rearrange("p o a n -> p (o a) n")
                            pool.tensor_tensor(kT[:, 2 * g:2 * g + 2, 0:WIN], kT[:, 2 * g:2 * g + 2, P:P + WIN], kept,
                                               ALU.mult).then_inc(s["tail_ready"], 1)
                        if last and u == 3:
                            break
                attention_bodies(pool, layer, body)

            def ffn_rstd(layer, kb):
                n = layer * BLOCKS + kb
                pool.wait_ge(s["f_mv"], n + 1)
                pool.tensor_tensor(vare[:, 0:4], mv[:, 0:4, 1], eps_row[:, 0:4], ALU.add).then_inc(s["f_ve"], 1)
                pool.wait_ge(s["f_ve"], n + 1)
                pool.tensor_tensor(rstd[:, 0:4], vare[:, 0:4], minus_half[:, 0:4], ALU.pow).then_inc(s["f_rstd"], 1)

            pool.wait_ge(s["pad_ready"], 1)
            with pool.Fori(0, DEPTH) as layer:
                attention(layer)
                with pool.Fori(0, BLOCKS) as kb:
                    ffn_rstd(layer, kb)

        @block.scalar
        def _(act):
            counts_of[act.engine] = [act.alloc_register(f"act_count{k}") for k in range(2)]
            act.preload_act_table_set("natural_log_exp_and_others")
            act.dma_start(wa[:, :, :], w_attn).then_inc(s["small_in"], 16)
            act.dma_start(wmod_sb[:, :], wmod).then_inc(s["small_in"], 16)
            act.dma_start(c_col[:, :], c_t).then_inc(s["small_in"], 16)
            act.dma_start(bqk_col[:, :], b_qk).then_inc(s["small_in"], 16)
            act.dma_start(bv_row[:, :], b_v.to_broadcast([P, D])).then_inc(s["small_in"], 16)
            act.dma_start(rot_raw[:, :, :, :, :], rot_tab).then_inc(s["gain_in"], 16)
            act.dma_start(qk_gain[:, :, :, :, :].rearrange("p l a b d -> p (l a b d)"),
                          gains.to_broadcast([P, DEPTH * 4 * DH])).then_inc(s["gain_in"], 16)
            act.dma_start(vec_cols[:, :, :], cols).then_inc(s["const_in"], 16)
            act.dma_start(b1_col[:, :, :, :], b1_cols).then_inc(s["const_in"], 16)

            act.wait_ge(s["small_in"], 16 * 5)
            act.activation(silu_t[:, 0, :], c_col[:, :], ACT.Exp, scale=-1.0).then_inc(s["silu_step"], 1)
            act.wait_ge(s["modp_ready"], 1)
            act.activation(mod_col[:, :, :], bank[0][:, 0:6 * B].rearrange("p (k b) -> p k b", b=B), ACT.Copy).then_inc(s["modp_ready"], 1)
            act.wait_ge(s["mod_ready"], 1)

            def norm_out(n, b, half, dst, k_scale_, k_shift):
                wait_apart(act, ("gtr_ready", n * 2 + half + 1))
                act.activation(dst, bank[half], ACT.Identity, scale=mod_col[:, k_scale_, bass.ds(b, 1)],
                               bias=mod_col[:, k_shift, bass.ds(b, 1)]).then_inc(s["gh_ready"], 1)

            with act.Fori(0, B) as b:
                for half in range(2):
                    norm_out(b * 2, b, half, hT[:, half * 512:half * 512 + 512], 1, 0)
                for n in range(4):
                    dst = (qT, kgT)[n // 2]
                    act.wait_ge(s["gq_ready"], b * 4 + n + 1)
                    act.activation(dst[:, n % 2 * 512:n % 2 * 512 + 512], bank[2 + n], ACT.Identity,
                                   bias=bqk_col[:, n // 2:n // 2 + 1]).then_inc(s["gqk_ready"], 1)
                for i in range(TPB):
                    n = b * TPB + i
                    act.wait_ge(s["gm_ready"], n + 1)
                    if i >= 2:
                        act.wait_ge(s["gt_ready"], n - 1)
                    act.activation(pg[:, i % 2, :].rearrange("p (a n) -> p a n", a=2), psum[:, i % 2 * 2:i % 2 * 2 + 2, :],
                                   ACT.Exp, bias=gmax[:, i % 2, 1:2], scale=float(D) ** -0.5,
                                   accum_out=gsum[:, i % 2, 0:1]).then_inc(s["ge_ready"], 1)
                    act.wait_ge(s["gt_ready"], n + 1)
                    need(act, "go_ready", b * TPB, i, False)
                    act.activation(pgT[:, 0:4, :], bank[4].rearrange("p (a n) -> p a n", a=4), ACT.Copy).then_inc(s["gte_a"], 1)
                for half in range(2):
                    norm_out(b * 2 + 1, b, half, xs_in[:, bass.ds(b * PITCH + HIST + half * 512, 512)], 4, 3)

            def attention(layer):
                def body(groups, it, first, last):
                    for u in range(UNROLL):
                        j = group_of(u, 4, first, last)
                        if j is not None:
                            need(act, "vp_ready", groups, j + 1)
                            need(act, "pv_ready", groups, j - 1, first)
                            act.activation(vs[:, j % 2, :, :, 0:DH].rearrange("p a b n -> p (a b) n"),
                                           bank[1][0:KEYS, :].rearrange("p (a n) -> p a n", n=DH), ACT.Copy).then_inc(s["vs_ready"], 1)
                        j = group_of(u, 5, first, last)
                        if j is not None:
                            need(act, "pt_ready", groups, j + 1)
                            need(act, "pv_ready", groups, j, first)
                            act.activation(probT[:, :, :], bank[4][0:KEYS, :].rearrange("p (a n) -> p a n", a=4),
                                           ACT.Copy).then_inc(s["pts_ready"], 1)
                        j = group_of(u, 2, first, last)
                        if j is not None:
                            g = j % GPT
                            need(act, "tr_ready", groups, j + 1)
                            need(act, "tail_ready", groups, j - GPT + 1, first)
                            need(act, "sim_ready", groups, j, first)
                            trq = bank[2][:, 0:256].rearrange("p (a n) -> p a n", n=DH)
                            act.activation(qbd[0:64, :, :, 0, :].rearrange("p a b n -> p (a b) n"), trq[0:64], ACT.Copy)
                            act.activation(qbd[64:P, :, :, 1, :].rearrange("p a b n -> p (a b) n"), trq[64:P], ACT.Copy)
                            act.activation(kT[:, 2 * g:2 * g + 2, WIN:WIN + P],
                                           bank[2][:, 256:512].rearrange("p (a n) -> p a n", a=2), ACT.Copy).then_inc(s["qk_ready"], 1)
                        j = group_of(u, 3, first, last)
                        if j is not None:
                            need(act, "max_ready", groups, j + 1)
                            need(act, "pn_ready", groups, j - 1, first)
                            for k in range(4):
                                ins = act.activation(prob[:, j % 2, k, :], bank[3][:, k * KEYS:(k + 1) * KEYS], ACT.Exp, bias=nmax[:, k:k + 1])
                            ins.then_inc(s["p_ready"], 1)
                        j = group_of(u, 0, first, last)
                        if j is not None:
                            need(act, "proj_ready", groups, j + 1)
                            need(act, "ss_ready", groups, j, first)
                            act.activation(sq[:, :, :], bank[6 * (j % 2)].rearrange("p (a n) -> p a n", n=DH), ACT.Square).then_inc(s["sq_ready"], 1)
                        j = group_of(u, 5, first, last)
                        if j is not None:
                            g, tp = j % GPT, j // GPT % 2
                            need(act, "pv_ready", groups, j + 1)
                            if g == 0:
                                need_tiles(act, "wo_ready", layer, it, j // GPT - 2, first, last)
                            act.activation(aoT[:, tp, 2 * g:2 * g + 2, :], bank[5][:, 0:256].rearrange("p (a n) -> p a n", a=2),
                                           ACT.Copy).then_inc(s["aot_ready"], 1)
                        j = group_of(u, 0, first, last)
                        if j is not None:
                            need(act, "sg_ready", groups, j + 1)
                            act.activation(lnss[:, :], ssg[:, :], ACT.Ln, scale=RN_SCALE * RN_SCALE).then_inc(s["ln_ready"], 1)
                            need(act, "ln_ready", groups, j + 1)
                            need(act, "qkn_ready", groups, j, first)
                            act.activation(rnorm[:, :], lnss[:, :], ACT.Exp, scale=-0.5).then_inc(s["rn_ready"], 1)
                        if last and u == 4:
                            break
                attention_bodies(act, layer, body)

            with act.Fori(0, DEPTH) as layer:
                act.preload_act_table_set("natural_log_exp_and_others")
                act.wait_ge(s["f_out"], layer * BLOCKS)
                attention(layer)
                act.preload_act_table(ACT.Gelu)
                act.wait_ge(s["const_in"], 16 * 2)

                def prep(kb):
                    n = layer * BLOCKS + kb
                    wait_apart(act, ("f_trn", n + 1))
                    act.activation(xnT[:, :], bank[1], ACT.Identity, scale=lng_col[:, bass.ds(layer, 1)],
                                   bias=lnb_col[:, bass.ds(layer, 1)]).then_inc(s["f_xnT"], 1)

                def main(kb, odd):
                    for ch in range(CH):
                        m = layer * BLOCKS * CH + kb * CH + ch
                        par = (odd * CH + ch) % 2
                        wait_apart(act, ("f_gate", m + 1), *([("f_u", m - 1)] if ch >= 2 or odd else []))
                        w = CW[ch]
                        act.activation(gel[0:w, par, :], bank[2 + par][0:w, :], ACT.Gelu,
                                       bias=b1_col[0:w, bass.ds(layer, 1), 1, ch]).then_inc(s["f_gel"], 1)
                prep(0)
                with act.Fori(0, BLOCKS // 2 - 1) as i:
                    for odd in range(2):
                        prep_main(act, prep, main, i * 2 + odd, odd)
                prep_main(act, prep, main, BLOCKS - 2, 0)
                main(BLOCKS - 1, 1)

        @block.tensor
        def _(pe):
            pe.wait_ge(s["silu_ready"], 1)
            pe.wait_ge(s["small_in"], 16 * 5)
            for k in range(6):
                mm = pe.matmul(bank[0][:, k * B:(k + 1) * B], wmod_sb[:, k * D:(k + 1) * D], silu_t[:, 2, :], start=True, stop=True)
            mm.then_inc(s["modp_ready"], 1)
            pe.wait_ge(s["wide_ready"], 1)
            for b in range(B):
                mm = pe.matmul(bank[1][:, b * D:(b + 1) * D], silu_wide[:, b, :], wmod_sb[:, 2 * D:3 * D], start=True, stop=True)
            mm.then_inc(s["gap_ready"], 1)
            pe.wait_ge(s["id_ready"], 1)
            pe.wait_ge(s["mod_ready"], 2)

            def norm_turn(n, half):
                if half == 0:
                    pe.wait_ge(s["gxn_ready"], n + 1)
                    pe.wait_ge(s["gh_ready"], n * 2)
                for i in range(4):
                    mm = pe.transpose(bank[half][:, i * P:(i + 1) * P], xn[:, half * 4 + i, :], ident[:, :])
                mm.then_inc(s["gtr_ready"], 1)

            with pe.Fori(0, B) as b:
                for half in range(2):
                    norm_turn(b * 2, half)
                for half in range(2):
                    pe.wait_ge(s["gh_ready"], b * 4 + half + 1)
                for n in range(4):
                    pe.matmul(bank[2 + n], wa[:, n // 2, :], hT[:, n % 2 * 512:n % 2 * 512 + 512], start=True, stop=True).then_inc(s["gq_ready"], 1)
                for half in range(2):
                    for i in range(4):
                        t = half * 4 + i
                        mm = pe.matmul(bank[6 + half][:, i * D:(i + 1) * D], hT[:, t * P:(t + 1) * P], wa[:, 2, :], start=True, stop=True)
                    mm.then_inc(s["gv_ready"], 1)
                for n in range(4):
                    pe.wait_ge(s["gqk_ready"], b * 4 + n + 1)

                def scores(i):
                    if i >= 2:
                        pe.wait_ge(s["ge_ready"], b * TPB + i - 1)
                    for half in range(2):
                        mm = pe.matmul(bank[i % 2 * 2 + half], qT[:, i * P:(i + 1) * P], kgT[:, half * 512:half * 512 + 512],
                                       start=True, stop=True)
                    mm.then_inc(s["gs_ready"], 1)

                def turn(i):
                    n = b * TPB + i
                    pe.wait_ge(s["ge_ready"], n + 1)
                    pe.wait_ge(s["gte_a"], n)
                    pe.wait_ge(s["gte_d"], n)
                    for k in range(TPB):
                        mm = pe.transpose(bank[4 + k // 4][:, k % 4 * P:k % 4 * P + P], pg[:, i % 2, k * P:(k + 1) * P], ident[:, :])
                    mm.then_inc(s["gt_ready"], 1)

                def values(i):
                    n = b * TPB + i
                    pe.wait_ge(s["gte_a"], n + 1)
                    pe.wait_ge(s["gte_d"], n + 1)
                    if i == 0:
                        pe.wait_ge(s["gvs_ready"], b * 2 + 2)
                    else:
                        pe.wait_ge(s["gx_ready"], n)
                    for k in range(TPB):
                        mm = pe.matmul(bank[6][:, 0:D], pgT[:, k, :], vg[:, k, :], start=(k == 0), stop=(k == TPB - 1))
                    mm.then_inc(s["go_ready"], 1)

                scores(0)
                for i in range(TPB):
                    if i + 1 < TPB:
                        scores(i + 1)
                    turn(i)
                    values(i)
                for half in range(2):
                    norm_turn(b * 2 + 1, half)

            def attention(layer):
                def body(groups, it, first, last):
                    for u in range(UNROLL):
                        j = group_of(u, 5, first, last)
                        if j is not None:
                            need(pe, "pn_ready", groups, j + 1)
                            need(pe, "pts_ready", groups, j, first)
                            for k in range(4):
                                mm = pe.transpose(bank[4][0:KEYS, k * P:(k + 1) * P], probn[:, k, :], ident[:, :])
                            mm.then_inc(s["pt_ready"], 1)
                        j = group_of(u, 2, first, last)
                        if j is not None:
                            need(pe, "qkr_ready", groups, j + 1)
                            need(pe, "qk_ready", groups, j, first)
                            for k in range(4):
                                mm = pe.transpose(bank[2][:, k * P:(k + 1) * P], qkr[:, k * P:(k + 1) * P], ident[:, :])
                            mm.then_inc(s["tr_ready"], 1)
                        j = group_of(u, 0, first, last)
                        if j is not None:
                            g, tp = j % GPT, j // GPT % 2
                            if g == 0:
                                need_tiles(pe, "xs_ready", layer, it, j // GPT, first, last)
                            need(pe, "qkn_ready", groups, j - 1, first)
                            for n, (xp, wp_) in enumerate(PARTS):
                                mm = pe.matmul(bank[6 * (j % 2)].rearrange("p (a n) -> p a n", a=2), xparts[xp][:, tp, WIN:WIN + P],
                                               wparts[wp_][:, 0:2, g * 256:(g + 1) * 256], start=(n == 0), stop=(n == 2))
                            mm.then_inc(s["proj_ready"], 1)
                        j = group_of(u, 5, first, last)
                        if j is not None:
                            need(pe, "pts_ready", groups, j + 1)
                            need(pe, "vs_ready", groups, j + 1)
                            need(pe, "aot_ready", groups, j, first)
                            for odd in range(2):
                                for h in (odd, 2 + odd):
                                    for wp in range(2):
                                        mm = pe.matmul(bank[5][odd * 64:odd * 64 + 64, h // 2 * P + wp * 64:h // 2 * P + wp * 64 + 64],
                                                       vs[:, j % 2, wp, h, :], probT[:, h // 2 * 2 + wp, odd * 64:odd * 64 + 64],
                                                       start=True, stop=True)
                            mm.then_inc(s["pv_ready"], 1)
                        j = group_of(u, 3, first, last)
                        if j is not None:
                            g, tp = j % GPT, j // GPT % 2
                            need(pe, "vs_ready", groups, j, first)
                            for wp in range(2):
                                for n, (xp, wp_) in enumerate(PARTS):
                                    mm = pe.matmul(bank[1][0:KEYS, wp * 256:(wp + 1) * 256], xparts[xp][:, tp, wp * 64:wp * 64 + KEYS],
                                                   wparts[wp_][:, 2, g * 256:(g + 1) * 256], start=(n == 0), stop=(n == 2))
                            mm.then_inc(s["vp_ready"], 1)
                        j = group_of(u, 6, first, last)
                        if j is not None and j % GPT == GPT - 1:
                            tp = j // GPT % 2
                            need(pe, "aot_ready", groups, j + 1)
                            need_tiles(pe, "x_mid_ready", layer, it, j // GPT - 1, first, last)
                            for k in range(INNER // P):
                                mm = pe.matmul(bank[7][:, 0:P], wo[:, k, :], aoT[:, tp, k, :], start=(k == 0), stop=(k == INNER // P - 1))
                            mm.then_inc(s["wo_ready"], 1)
                        j = group_of(u, 2, first, last)
                        if j is not None:
                            g, tp = j % GPT, j // GPT % 2
                            need(pe, "qk_ready", groups, j + 1)
                            need(pe, "p_ready", groups, j, first)
                            entry = 1 if tp else (it if isinstance(it, int) else pe.snap(it % 4))
                            m = mask[:, bass.ds(entry, 1), :, :].rearrange("p a b k -> p (a b) k").unsqueeze(1).to_broadcast([P, 2, 2, KEYS])
                            pe.matmul(bank[3][:, 0:4 * KEYS].rearrange("p (a b k) -> p a b k", a=2, b=2), ident_bf[:, :], m,
                                      start=True, stop=False, skip_group_check=True)
                            for hp in range(2):
                                for wp in range(2):
                                    k = hp * 2 + wp
                                    mm = pe.matmul(bank[3][:, k * KEYS:(k + 1) * KEYS],
                                                   qbd[:, hp, wp, :, :].rearrange("p a n -> p (a n)"),
                                                   kT[:, 2 * g + hp, wp * 64:wp * 64 + KEYS], start=False, stop=(k == 3),
                                                   skip_group_check=True)
                            mm.then_inc(s["sim_ready"], 1)
                        if last and u == 5:
                            break
                attention_bodies(pe, layer, body)

            pe.wait_ge(s["mask_ready"], 6)
            pe.wait_ge(s["pad_ready"], 1)
            with pe.Fori(0, DEPTH) as layer:
                pe.wait_ge(s["f_out"], layer * BLOCKS)
                pe.wait_ge(s["w_split"], layer * 2 + 2)
                pe.wait_ge(s["wo_in"], layer * 16 + 16)
                attention(layer)
                pe.wait_ge(s["w1_in"], layer * 16 + 16)
                pe.wait_ge(s["w2_in"], layer * 16 + 16)

                def turn_in(kb):
                    n = layer * BLOCKS + kb
                    pe.wait_ge(s["f_x"], (n + 1) * 32)
                    pe.wait_ge(s["f_xn"], n)
                    for i in range(4):
                        mm = pe.transpose(bank[0][:, i * P:(i + 1) * P], xf[:, i * P:(i + 1) * P], ident[:, :])
                    mm.then_inc(s["f_tr"], 1)

                def turn_back(kb):
                    n = layer * BLOCKS + kb
                    pe.wait_ge(s["f_xn"], n + 1)
                    for i in range(4):
                        mm = pe.transpose(bank[1][:, i * P:(i + 1) * P], xn[:, i, :], ident[:, :])
                    mm.then_inc(s["f_trn"], 1)

                def prep(kb):
                    turn_in(kb)
                    turn_back(kb)

                def up(kb, odd):
                    n = layer * BLOCKS + kb
                    pe.wait_ge(s["f_xnT"], n + 1)
                    for ch in range(CH):
                        m = n * CH + ch
                        par = (odd * CH + ch) % 2
                        w = CW[ch]
                        if ch >= 2 or odd:
                            pe.wait_ge(s["f_gel"], m - 1)
                        pe.matmul(bank[2 + par][0:w, :], w1[:, DFF + ch * P:DFF + ch * P + w], xnT[:, :], start=True, stop=True).then_inc(s["f_gate"], 1)
                        if ch >= 2 or odd:
                            pe.wait_ge(s["f_u"], m - 1)
                        pe.matmul(bank[4 + par][0:w, :], w1[:, ch * P:ch * P + w], xnT[:, :], start=True, stop=True).then_inc(s["f_a"], 1)

                def down(kb):
                    n = layer * BLOCKS + kb
                    pe.wait_ge(s["f_out"], n)
                    for ch in range(CH):
                        pe.wait_ge(s["f_u"], n * CH + ch + 1)
                        mm = pe.matmul(bank[6], w2[:, ch, :], uT[:, ch, :], start=(ch == 0), stop=(ch == CH - 1))
                    mm.then_inc(s["f_y"], 1)

                def step(kb, odd):
                    turn_in(kb + 1)
                    up(kb, odd)
                    turn_back(kb + 1)
                    down(kb)
                prep(0)
                with pe.Fori(0, BLOCKS // 2 - 1) as i:
                    for odd in range(2):
                        step(i * 2 + odd, odd)
                step(BLOCKS - 2, 0)
                up(BLOCKS - 1, 1)
                down(BLOCKS - 1)
            with pe.Fori(0, BLOCKS // 2) as i:
                for h in range(2):
                    n = i * 2 + h
                    pe.wait_ge(s["y_ready"], n + 1)
                    if h == 0:
                        pe.wait_ge(s["yo_ready"], n)
                    for k in range(4):
                        mm = pe.transpose(bank[h][:, k * P:(k + 1) * P], yT[:, h, k * P:(k + 1) * P], ident[:, :])
                    mm.then_inc(s["y_tr"], 1)

        @block.vector
        def _(dve):
            counts_of[dve.engine] = [dve.alloc_register(f"dve_count{k}") for k in range(2)]
            dve.wait_ge(s["silu_step"], 1)
            dve.tensor_scalar(silu_t[:, 1, :], silu_t[:, 0, :], 1.0, None, ALU.add).then_inc(s["silu_step"], 1)
            dve.wait_ge(s["silu_step"], 2)
            dve.reciprocal(silu_t[:, 0, :], silu_t[:, 1, :]).then_inc(s["silu_step"], 1)
            dve.wait_ge(s["silu_step"], 3)
            dve.tensor_tensor(silu_t[:, 2, :], silu_t[:, 0, :], c_col[:, :], ALU.mult).then_inc(s["silu_ready"], 1)
            dve.wait_ge(s["silu_ready"], 1)
            dve.tensor_copy(silu_wide[:, :, :], silu_t[:, 2, :].unsqueeze(2).to_broadcast([P, B, P])).then_inc(s["wide_ready"], 1)

            steps = [0]

            def clamp(dst, src, tmp):
                dve.tensor_scalar(tmp[0], src, 0.0, 2.0, ALU.is_ge, ALU.mult).then_inc(s["clamp_step"], 1)
                dve.scalar_tensor_tensor(out=tmp[1], in0=src, scalar=-1.0, in1=src, op0=ALU.mult, op1=ALU.max).then_inc(s["clamp_step"], 1)
                steps[0] += 2
                dve.wait_ge(s["clamp_step"], steps[0])
                dve.tensor_scalar(tmp[1], tmp[1], 0.25, None, ALU.max).then_inc(s["clamp_step"], 1)
                steps[0] += 1
                dve.wait_ge(s["clamp_step"], steps[0])
                return dve.scalar_tensor_tensor(out=dst, in0=tmp[0], scalar=-1.0, in1=tmp[1], op0=ALU.add, op1=ALU.mult)

            dve.wait_ge(s["modp_ready"], 2)
            dve.tensor_scalar(mod_col[:, 1, :], mod_col[:, 1, :], 1.0, None, ALU.add)
            dve.tensor_scalar(mod_col[:, 4, :], mod_col[:, 4, :], 1.0, None, ALU.add)
            clamp(mod_col[:, 5, :], mod_col[:, 5, :], [clamp_c[:, 0, :], clamp_c[:, 1, :]]).then_inc(s["mod_ready"], 1)
            dve.wait_ge(s["gap_ready"], 1)
            dve.tensor_copy(ga_row[:, :, :].rearrange("p b d -> p (b d)"), bank[1]).then_inc(s["clamp_step"], 1)
            steps[0] += 1
            dve.wait_ge(s["clamp_step"], steps[0])
            clamp(ga_row[:, :, :].rearrange("p b d -> p (b d)"), ga_row[:, :, :].rearrange("p b d -> p (b d)"), [clamp_t[:, 0, :], clamp_t[:, 1, :]]).then_inc(s["mod_ready"], 1)
            dve.wait_ge(s["mod_ready"], 2)
            dve.wait_ge(s["x_in"], 16 * B)

            def norm_tiles(n, b):
                for i in range(TPB):
                    dve.bn_stats(st6[:, i, :], xtok[:, bass.ds(b * TPB + i, 1), :].rearrange("p a d -> p (a d)")).then_inc(s["gst_step"], 1)
                for i in range(TPB):
                    if i == 0:
                        wait_apart(dve, ("gst_step", n * TPB + TPB))
                    ins = dve.bn_aggr(mv[:, i, :], st6[:, i, :])
                ins.then_inc(s["gmv_ready"], 1)
                dve.wait_ge(s["grstd_ready"], n + 1)
                dve.wait_ge(s["gtr_ready"], n * 2)
                for i in range(TPB):
                    ins = dve.tensor_scalar(xn[:, i, :], xtok[:, bass.ds(b * TPB + i, 1), :].rearrange("p a d -> p (a d)"),
                                            mv[:, i, 0:1], rstd[:, i:i + 1], ALU.subtract, ALU.mult)
                ins.then_inc(s["gxn_ready"], 1)

            with dve.Fori(0, B) as b:
                norm_tiles(b * 2, b)
                for half in range(2):
                    n = b * 2 + half
                    dve.wait_ge(s["gv_ready"], n + 1)
                    v = vg[:, half * 4:half * 4 + 4, :]
                    dve.tensor_tensor(v, bank[6 + half].rearrange("p (a d) -> p a d", a=4),
                                      bv_row[:, :].unsqueeze(1).to_broadcast([P, 4, D]), ALU.add).then_inc(s["gvt_step"], 1)
                    dve.wait_ge(s["gvt_step"], n + 1)
                    dve.tensor_tensor(v, v, ga_row[:, bass.ds(b, 1), :].to_broadcast([P, 4, D]), ALU.mult).then_inc(s["gvs_ready"], 1)

                def row_max(i):
                    n = b * TPB + i
                    dve.wait_ge(s["gs_ready"], n + 1)
                    dve.tensor_reduce(gmax[:, i % 2, 0:1], psum[:, i % 2 * 2:i % 2 * 2 + 2, :], AX.XY, ALU.max, negate=True).then_inc(s["gm_step"], 1)
                    dve.wait_ge(s["gm_step"], n + 1)
                    dve.tensor_scalar(gmax[:, i % 2, 1:2], gmax[:, i % 2, 0:1], float(D) ** -0.5, None, ALU.mult).then_inc(s["gm_ready"], 1)

                row_max(0)
                for i in range(TPB):
                    n = b * TPB + i
                    if i + 1 < TPB:
                        row_max(i + 1)
                    dve.wait_ge(s["gt_ready"], n + 1)
                    dve.wait_ge(s["go_ready"], n)
                    dve.tensor_copy(pgT[:, 4:8, :], bank[5].rearrange("p (a n) -> p a n", a=4)).then_inc(s["gte_d"], 1)
                    dve.wait_ge(s["ge_ready"], n + 1)
                    dve.reciprocal(gsum[:, i % 2, 1:2], gsum[:, i % 2, 0:1]).then_inc(s["gri_step"], 1)
                    dve.wait_ge(s["gri_step"], n + 1)
                    dve.wait_ge(s["go_ready"], n + 1)
                    xt = xtok[:, bass.ds(n, 1), :].rearrange("p a d -> p (a d)")
                    dve.scalar_tensor_tensor(out=xt, in0=bank[6][:, 0:D], scalar=gsum[:, i % 2, 1:2], in1=xt,
                                             op0=ALU.mult, op1=ALU.add).then_inc(s["gx_ready"], 1)
                wait_apart(dve, ("gx_ready", b * TPB + TPB))
                norm_tiles(b * 2 + 1, b)

            def attention(layer):
                def body(groups, it, first, last):
                    for u in range(UNROLL):
                        if u % GPT == 0 and not last:
                            tp = u // GPT
                            dve.wait_ge(xsh_in[tp], (layer * ITERS + it + 1) * 32)
                            need(dve, "vp_ready", groups, u - GPT, first)
                            dve.tensor_copy(xhi[:, tp, :], xsh[:, tp, :]).then_inc(s["xh_step"], 1)
                            dve.wait_ge(s["xh_step"], layer * TILES + it * 2 + (tp + 1))
                            dve.tensor_tensor(xlo[:, tp, :], xsh[:, tp, :], xhi[:, tp, :].bitcast(F32), ALU.subtract).then_inc(s["xs_ready"], 1)
                        j = group_of(u, 4, first, last)
                        if j is not None:
                            need(dve, "p_ready", groups, j + 1)
                            need(dve, "pn_ready", groups, j - 1, first)
                            dve.tensor_reduce(psumr[:, j % 2, 0, :], prob[:, j % 2, :, :], AX.X, ALU.add).then_inc(s["sum_ready"], 1)
                            need(dve, "sum_ready", groups, j + 1)
                            dve.reciprocal(psumr[:, j % 2, 1, :], psumr[:, j % 2, 0, :]).then_inc(s["ri_ready"], 1)
                        j = group_of(u, 1, first, last)
                        if j is not None:
                            need(dve, "rn_ready", groups, j + 1)
                            need(dve, "rot_ready", groups, j, first)
                            dve.tensor_tensor(qkn[:, :, :], bank[6 * (j % 2)].rearrange("p (a n) -> p a n", n=DH),
                                              rnorm[:, :].unsqueeze(2).to_broadcast([P, 8, DH]), ALU.mult).then_inc(s["qkn_ready"], 1)
                        j = group_of(u, 1, first, last)
                        if j is not None:
                            if isinstance(it, int):
                                t8 = (j // GPT) % TPB
                            else:
                                t8 = dve.snap((it * 2 + (j // GPT) % TPB) % TPB)
                            H = DH // 2
                            need(dve, "qkn_ready", groups, j + 1)
                            need(dve, "qkr_ready", groups, j, first)
                            x4 = qkn[:, :, :].rearrange("p (a h) d -> p a h d", a=2)

                            def table(k, lo, n):
                                t = rot[:, k, bass.ds(t8, 1), :, lo:lo + n].rearrange("p o a d -> p (o a) d")
                                return t.unsqueeze(2).to_broadcast([P, 2, 4, n])
                            rc = rcos[:, :, :].rearrange("p (a h) d -> p a h d", a=2)
                            rs = rsin[:, :, :].rearrange("p (a h) d -> p a h d", a=2)
                            dve.tensor_tensor(rc, x4, table(0, 0, DH), ALU.mult)
                            dve.tensor_tensor(rs[:, :, :, 0:H], x4[:, :, :, H:DH], table(1, 0, H), ALU.mult)
                            dve.tensor_tensor(rs[:, :, :, H:DH], x4[:, :, :, 0:H], table(1, H, H), ALU.mult).then_inc(s["rot_ready"], 1)
                        j = group_of(u, 0, first, last)
                        if j is not None:
                            need(dve, "sq_ready", groups, j + 1)
                            dve.tensor_reduce(ssq[:, :], sq[:, :, :], AX.X, ALU.add).then_inc(s["ss_ready"], 1)
                            need(dve, "ss_ready", groups, j + 1)
                            need(dve, "ln_ready", groups, j, first)
                            dve.tensor_scalar(ssg[:, :], ssq[:, :], 1e-24, None, ALU.max).then_inc(s["sg_ready"], 1)
                        j = group_of(u, 2, first, last)
                        if j is not None:
                            need(dve, "sim_ready", groups, j + 1)
                            need(dve, "p_ready", groups, j, first)
                            dve.tensor_reduce(nmax[:, :], bank[3][:, 0:4 * KEYS].rearrange("p (a k) -> p a k", k=KEYS), AX.X, ALU.max,
                                              negate=True).then_inc(s["max_ready"], 1)
                        j = group_of(u, 7, first, last)
                        if j is not None and j % GPT == GPT - 1:
                            tile_off = j // GPT
                            need_tiles(dve, "wo_ready", layer, it, tile_off, first, last)
                            ip = ITERS if last else it
                            col = ip * (2 * P) + tile_off * P + (ip - 1) // (TPB // 2)
                            if not last:
                                col = dve.snap(col)
                            dve.tensor_tensor(x_mid[:, bass.ds(col + 1, P)], bank[7][:, 0:P], xs_in[:, bass.ds(col + HIST, P)],
                                              ALU.add).then_inc(s["x_mid_ready"], 1)
                        if last and u == 6:
                            break
                attention_bodies(dve, layer, body)

            dve.wait_ge(s["gain_in"], 16 * 2)
            dve.wait_ge(s["const_in"], 16 * 2)
            dve.wait_ge(s["gh_ready"], 4 * B)
            with dve.Fori(0, DEPTH) as layer:
                for k in range(2):
                    for n in range(2):
                        ins = dve.tensor_tensor(rot[:, k, :, n, :], rot_raw[:, :, k, n, :],
                                                qk_gain[:, bass.ds(layer, 1), k, n, :].to_broadcast([P, TPB, DH]), ALU.mult)
                ins.then_inc(s["gain_ready"], 1)
                dve.wait_ge(s["gain_ready"], layer + 1)
                dve.wait_ge(s["wqkv_in"], layer * 16 + 16)
                dve.tensor_copy(whi[:, :, :], wqkv[:, :, :]).then_inc(s["w_split"], 1)
                dve.wait_ge(s["w_split"], layer * 2 + 1)
                dve.tensor_tensor(wlo[:, :, :], wqkv[:, :, :], whi[:, :, :].bitcast(F32), ALU.subtract).then_inc(s["w_split"], 1)
                attention(layer)

                def stats(kb):
                    n = layer * BLOCKS + kb
                    dve.wait_ge(s["f_tr"], n + 1)
                    for i in range(4):
                        ins = dve.bn_stats(st6[:, i, :], bank[0][:, i * P:(i + 1) * P])
                    ins.then_inc(s["f_mvs"], 1)
                    wait_apart(dve, ("f_mvs", n + 1))
                    for i in range(4):
                        ins = dve.bn_aggr(mv[:, i, :], st6[:, i, :])
                    ins.then_inc(s["f_mv"], 1)

                def normalise(kb):
                    n = layer * BLOCKS + kb
                    dve.wait_ge(s["f_rstd"], n + 1)
                    dve.wait_ge(s["f_trn"], n)
                    for i in range(4):
                        ins = dve.tensor_scalar(xn[:, i, :], bank[0][:, i * P:(i + 1) * P], mv[:, i, 0:1], rstd[:, i:i + 1],
                                                ALU.subtract, ALU.mult)
                    ins.then_inc(s["f_xn"], 1)

                def prep(kb):
                    stats(kb)
                    normalise(kb)

                def gated(kb, odd, ch):
                    m = layer * BLOCKS * CH + kb * CH + ch
                    par = (odd * CH + ch) % 2
                    w = CW[ch]
                    if ch == 0:
                        dve.wait_ge(s["f_y"], layer * BLOCKS + kb)
                    dve.wait_ge(s["f_a"], m + 1)
                    dve.wait_ge(s["f_gel"], m + 1)
                    dve.scalar_tensor_tensor(out=uT[0:w, ch, :], in0=bank[4 + par][0:w, :], scalar=b1_col[0:w, bass.ds(layer, 1), 0, ch],
                                             in1=gel[0:w, par, :], op0=ALU.add, op1=ALU.mult).then_inc(s["f_u"], 1)

                def finish(kb):
                    n = layer * BLOCKS + kb
                    dve.wait_ge(s["f_y"], n + 1)
                    dve.scalar_tensor_tensor(out=xs_in[:, bass.ds(kb * BLK + kb // 2 + HIST, BLK)], in0=bank[6], scalar=b2_col[:, bass.ds(layer, 1)],
                                             in1=x_mid[:, bass.ds(kb * BLK + kb // 2 + 1, BLK)], op0=ALU.add, op1=ALU.add).then_inc(s["f_out"], 1)

                def step(kb, odd):
                    stats(kb + 1)
                    gated(kb, odd, 0)
                    normalise(kb + 1)
                    gated(kb, odd, 1)
                    gated(kb, odd, 2)
                    finish(kb)
                prep(0)
                with dve.Fori(0, BLOCKS // 2 - 1) as i:
                    for odd in range(2):
                        step(i * 2 + odd, odd)
                step(BLOCKS - 2, 0)
                for ch in range(CH):
                    gated(BLOCKS - 1, 1, ch)
                finish(BLOCKS - 1)

            with dve.Fori(0, BLOCKS // 2) as i:
                for h in range(2):
                    n = i * 2 + h
                    dve.wait_ge(s["f_out"], DEPTH * BLOCKS)
                    dve.wait_ge(s["y_tr"], i * 2 + 0)
                    dve.tensor_scalar(yT[:, h, :], xs_in[:, bass.ds(n * BLK + i + HIST, BLK)], mod_col[:, 5, bass.ds(i, 1)], None,
                                      ALU.mult).then_inc(s["y_ready"], 1)
                for h in range(2):
                    n = i * 2 + h
                    dve.wait_ge(s["y_tr"], n + 1)
                    dve.wait_ge(s["y_sent"], i * 32)
                    dve.tensor_tensor(yout[:, h, :, :], bank[h].rearrange("p (a d) -> p a d", a=4),
                                      xtok[:, bass.ds(n * 4, 4), :], ALU.add).then_inc(s["yo_ready"], 1)


def rotary_tables():
    import numpy as np
    f = np.float32
    half = np.arange(0, DH, 2, dtype=f)
    inv_freq = (f(1.0) / np.power(f(10000.0), half / f(DH))).astype(f)
    t = np.arange(S, dtype=f)
    freqs = (t[:, None] * inv_freq[None, :]).astype(f)
    base = ((half + f(0.4 * DH)) / f(1.4 * DH)).astype(f)
    power = ((t - f(S // 2)) / f(WIN // 2)).astype(f)
    scale = np.power(base[None, :].astype(np.float64), power[:, None]).astype(f)
    cos, sin = np.cos(freqs.astype(np.float64)).astype(f), np.sin(freqs.astype(np.float64)).astype(f)
    tab = np.zeros((S, 2, 2, DH), f)
    for n, m in enumerate((scale * f(QK_SCALE * RN_SCALE), (f(1.0) / scale) * f(RN_SCALE))):
        tab[:, 0, n, :] = np.concatenate([cos * m, cos * m], -1)
        tab[:, 1, n, :] = np.concatenate([-sin * m, sin * m], -1)
    return np.ascontiguousarray(tab.reshape(TPB, P, 2, 2, DH).transpose(1, 0, 2, 3, 4))


def kernel(**inputs):
    import numpy as _np
    import concourse.bacc as _bacc
    from concourse import mybir as _mybir
    from concourse.bass_utils import run_bass_kernel_spmd as _run

    a = {k.split("_", 2)[-1]: _np.asarray(v) for k, v in inputs.items()}
    f = _np.float32
    b1 = _np.zeros((2, CH * P, DEPTH), f)
    b1[:, :DFF] = a["b1"].reshape(DEPTH, 2, DFF).transpose(1, 2, 0)
    w2 = _np.zeros((DEPTH, CH * P, D), f)
    w2[:, :DFF] = a["W2"]
    gain = _np.stack([a["q_scale"], a["k_scale"]], 1)
    swapped = _np.concatenate([gain[..., DH // 2:], gain[..., :DH // 2]], -1)
    data = {
        "x": a["x"],
        "w_attn": _np.stack([a["Wq"], a["Wk"], a["Wv"]], 1),
        "b_qk": _np.stack([a["bq"], a["bk"]], 1),
        "b_v": a["bv"].reshape(1, D),
        "Wqkv": a["Wqkv"],
        "Wo": a["Wo"].reshape(DEPTH, INNER // P, P, D).transpose(0, 2, 1, 3).reshape(DEPTH, P, INNER),
        "W1": a["W1"],
        "W2": w2.reshape(DEPTH, CH, P, D).transpose(0, 2, 1, 3).reshape(DEPTH, P, CH * D),
        "cols": _np.stack([a["ln_g"].T, a["ln_b"].T, a["b2"].T], 1),
        "b1_cols": b1.reshape(2, CH, P, DEPTH).transpose(2, 3, 0, 1),
        "gains": _np.stack([gain, swapped], 1).reshape(1, -1),
        "c_t": inputs["L0_c"].T,
        "wmod": inputs["L0_wmod"],
        "rot_tab": rotary_tables(),
    }
    nc = _bacc.Bacc("TRN2", target_bir_lowering=False, num_devices=1)
    arrays, args = {}, []
    for name, v in data.items():
        v = _np.ascontiguousarray(v)
        arrays[name + "_dram"] = v
        args.append(nc.dram_tensor(name + "_dram", v.shape, _mybir.dt.from_np(v.dtype), kind="ExternalInput").ap())
    o = nc.dram_tensor("out_0_dram", (B, S, D), F32, kind="ExternalOutput").ap()
    build(nc, *args, o)
    r = _run(nc, [arrays], core_ids=[0])
    return r.results[0]["out_0_dram"]
```
